# Optimizing a Trainium2 kernel written in Bass

```python
import numpy as np
import jax
import jax.numpy as jnp

def _softmax(x, axis=-1):
    return jax.nn.softmax(x, axis=axis)

def _gelu(x):
    return jax.nn.gelu(x, approximate=True)

def _silu(x):
    return jax.nn.silu(x)

def _sigmoid(x):
    return jax.nn.sigmoid(x)

def _layernorm(x, axis=-1, eps=1e-05):
    m = jnp.mean(x, axis=axis, keepdims=True)
    v = jnp.var(x, axis=axis, keepdims=True)
    return (x - m) / jnp.sqrt(v + eps)

def _scatter_add(tgt, idx, src, axis=0):
    return tgt.at[idx].add(src)

def _segment_sum(src, seg, n):
    return jax.ops.segment_sum(src, seg, n)
kernel_name = 'mk_dlrm_tower_d1_rec_r8_c4142b'

def setup_inputs(seed: int=0):
    np.random.seed(seed)
    _w = jnp.asarray

    def _rec_inputs():
        import jax
        import jax.numpy as jnp
        _tk = jax.random.key(seed)
        dense_ctx = jax.random.normal(jax.random.fold_in(_tk, 190), (2048, 16), jnp.float32)
        ids = jnp.stack([jax.random.randint(jax.random.fold_in(_tk, 200 + f), (2048,), 0, v, jnp.int32) for f, v in enumerate([1250, 1250, 125000, 1250, 1000, 1000, 12500, 1250, 1000, 12500, 1000, 1000, 12500, 1250, 1250, 1250, 12500, 1000, 12500, 12500, 1000, 12500, 1250, 1000, 1000, 1000, 12500])], axis=1)
        tbl_0 = 0.05 * jax.random.normal(jax.random.fold_in(_tk, 500 + 0), (1250, 128), jnp.float32)
        tbl_1 = 0.05 * jax.random.normal(jax.random.fold_in(_tk, 500 + 1), (1250, 128), jnp.float32)
        tbl_2 = 0.05 * jax.random.normal(jax.random.fold_in(_tk, 500 + 2), (125000, 128), jnp.float32)
        tbl_3 = 0.05 * jax.random.normal(jax.random.fold_in(_tk, 500 + 3), (1250, 128), jnp.float32)
        tbl_4 = 0.05 * jax.random.normal(jax.random.fold_in(_tk, 500 + 4), (1000, 128), jnp.float32)
        tbl_5 = 0.05 * jax.random.normal(jax.random.fold_in(_tk, 500 + 5), (1000, 128), jnp.float32)
        tbl_6 = 0.05 * jax.random.normal(jax.random.fold_in(_tk, 500 + 6), (12500, 128), jnp.float32)
        tbl_7 = 0.05 * jax.random.normal(jax.random.fold_in(_tk, 500 + 7), (1250, 128), jnp.float32)
        tbl_8 = 0.05 * jax.random.normal(jax.random.fold_in(_tk, 500 + 8), (1000, 128), jnp.float32)
        tbl_9 = 0.05 * jax.random.normal(jax.random.fold_in(_tk, 500 + 9), (12500, 128), jnp.float32)
        tbl_10 = 0.05 * jax.random.normal(jax.random.fold_in(_tk, 500 + 10), (1000, 128), jnp.float32)
        tbl_11 = 0.05 * jax.random.normal(jax.random.fold_in(_tk, 500 + 11), (1000, 128), jnp.float32)
        tbl_12 = 0.05 * jax.random.normal(jax.random.fold_in(_tk, 500 + 12), (12500, 128), jnp.float32)
        tbl_13 = 0.05 * jax.random.normal(jax.random.fold_in(_tk, 500 + 13), (1250, 128), jnp.float32)
        tbl_14 = 0.05 * jax.random.normal(jax.random.fold_in(_tk, 500 + 14), (1250, 128), jnp.float32)
        tbl_15 = 0.05 * jax.random.normal(jax.random.fold_in(_tk, 500 + 15), (1250, 128), jnp.float32)
        tbl_16 = 0.05 * jax.random.normal(jax.random.fold_in(_tk, 500 + 16), (12500, 128), jnp.float32)
        tbl_17 = 0.05 * jax.random.normal(jax.random.fold_in(_tk, 500 + 17), (1000, 128), jnp.float32)
        tbl_18 = 0.05 * jax.random.normal(jax.random.fold_in(_tk, 500 + 18), (12500, 128), jnp.float32)
        tbl_19 = 0.05 * jax.random.normal(jax.random.fold_in(_tk, 500 + 19), (12500, 128), jnp.float32)
        tbl_20 = 0.05 * jax.random.normal(jax.random.fold_in(_tk, 500 + 20), (1000, 128), jnp.float32)
        tbl_21 = 0.05 * jax.random.normal(jax.random.fold_in(_tk, 500 + 21), (12500, 128), jnp.float32)
        tbl_22 = 0.05 * jax.random.normal(jax.random.fold_in(_tk, 500 + 22), (1250, 128), jnp.float32)
        tbl_23 = 0.05 * jax.random.normal(jax.random.fold_in(_tk, 500 + 23), (1000, 128), jnp.float32)
        tbl_24 = 0.05 * jax.random.normal(jax.random.fold_in(_tk, 500 + 24), (1000, 128), jnp.float32)
        tbl_25 = 0.05 * jax.random.normal(jax.random.fold_in(_tk, 500 + 25), (1000, 128), jnp.float32)
        tbl_26 = 0.05 * jax.random.normal(jax.random.fold_in(_tk, 500 + 26), (12500, 128), jnp.float32)
        _rk = jax.random.fold_in(_tk, 7)
        W_top1 = 0.0521996 * jax.random.normal(jax.random.fold_in(_tk, 801), (367, 512), jnp.float32)
        W_top2 = 0.0441942 * jax.random.normal(jax.random.fold_in(_tk, 802), (512, 256), jnp.float32)
        W_top3 = 0.0625 * jax.random.normal(jax.random.fold_in(_tk, 803), (256, 1), jnp.float32)
        b_top1 = jnp.zeros((512,), jnp.float32)
        b_top2 = jnp.zeros((256,), jnp.float32)
        return (dense_ctx, ids, tbl_0, tbl_1, tbl_2, tbl_3, tbl_4, tbl_5, tbl_6, tbl_7, tbl_8, tbl_9, tbl_10, tbl_11, tbl_12, tbl_13, tbl_14, tbl_15, tbl_16, tbl_17, tbl_18, tbl_19, tbl_20, tbl_21, tbl_22, tbl_23, tbl_24, tbl_25, tbl_26, W_top1, b_top1, W_top2, b_top2, W_top3)
    dense_ctx, ids, tbl_0, tbl_1, tbl_2, tbl_3, tbl_4, tbl_5, tbl_6, tbl_7, tbl_8, tbl_9, tbl_10, tbl_11, tbl_12, tbl_13, tbl_14, tbl_15, tbl_16, tbl_17, tbl_18, tbl_19, tbl_20, tbl_21, tbl_22, tbl_23, tbl_24, tbl_25, tbl_26, W_top1, b_top1, W_top2, b_top2, W_top3 = _rec_inputs()

    def _L0_rec_setup():
        import jax, jax.numpy as jnp
        import numpy as np

        def _tri_indices(num_feas):
            return np.array([i * num_feas + j for j in range(1, num_feas) for i in range(j)], dtype=np.int32)
        key = jax.random.key(seed)
        batch, num_feas, embed_dim = (2048, 27, 128)
        inputs = jax.random.normal(key, (batch, num_feas, embed_dim), dtype=jnp.float32)
        return {'inputs': inputs, 'num_feas': num_feas}
    _L0_rec_all = _L0_rec_setup()
    _L0_rec_in = {k: v for k, v in _L0_rec_all.items() if k in ()}
    del _L0_rec_all
    return {'dense_ctx': dense_ctx, 'ids': ids, 'tbl_0': tbl_0, 'tbl_1': tbl_1, 'tbl_2': tbl_2, 'tbl_3': tbl_3, 'tbl_4': tbl_4, 'tbl_5': tbl_5, 'tbl_6': tbl_6, 'tbl_7': tbl_7, 'tbl_8': tbl_8, 'tbl_9': tbl_9, 'tbl_10': tbl_10, 'tbl_11': tbl_11, 'tbl_12': tbl_12, 'tbl_13': tbl_13, 'tbl_14': tbl_14, 'tbl_15': tbl_15, 'tbl_16': tbl_16, 'tbl_17': tbl_17, 'tbl_18': tbl_18, 'tbl_19': tbl_19, 'tbl_20': tbl_20, 'tbl_21': tbl_21, 'tbl_22': tbl_22, 'tbl_23': tbl_23, 'tbl_24': tbl_24, 'tbl_25': tbl_25, 'tbl_26': tbl_26, 'W_top1': W_top1, 'b_top1': b_top1, 'W_top2': W_top2, 'b_top2': b_top2, 'W_top3': W_top3}

def reference(dense_ctx, ids, tbl_0, tbl_1, tbl_2, tbl_3, tbl_4, tbl_5, tbl_6, tbl_7, tbl_8, tbl_9, tbl_10, tbl_11, tbl_12, tbl_13, tbl_14, tbl_15, tbl_16, tbl_17, tbl_18, tbl_19, tbl_20, tbl_21, tbl_22, tbl_23, tbl_24, tbl_25, tbl_26, W_top1, b_top1, W_top2, b_top2, W_top3):
    import jax
    import jax.numpy as jnp

    def _L0_rec_ref(inputs, num_feas):
        import jax, jax.numpy as jnp
        import numpy as np

        def _tri_indices(num_feas):
            return np.array([i * num_feas + j for j in range(1, num_feas) for i in range(j)], dtype=np.int32)
        dot = jnp.einsum('bnd,bmd->bnm', inputs, inputs)
        idx = jnp.asarray(_tri_indices(num_feas))
        flat = dot.reshape(inputs.shape[0], num_feas * num_feas)
        return flat[:, idx]
    e = jnp.stack([tbl_0[ids[:, 0]], tbl_1[ids[:, 1]], tbl_2[ids[:, 2]], tbl_3[ids[:, 3]], tbl_4[ids[:, 4]], tbl_5[ids[:, 5]], tbl_6[ids[:, 6]], tbl_7[ids[:, 7]], tbl_8[ids[:, 8]], tbl_9[ids[:, 9]], tbl_10[ids[:, 10]], tbl_11[ids[:, 11]], tbl_12[ids[:, 12]], tbl_13[ids[:, 13]], tbl_14[ids[:, 14]], tbl_15[ids[:, 15]], tbl_16[ids[:, 16]], tbl_17[ids[:, 17]], tbl_18[ids[:, 18]], tbl_19[ids[:, 19]], tbl_20[ids[:, 20]], tbl_21[ids[:, 21]], tbl_22[ids[:, 22]], tbl_23[ids[:, 23]], tbl_24[ids[:, 24]], tbl_25[ids[:, 25]], tbl_26[ids[:, 26]]], axis=1)
    z = _L0_rec_ref(e, 27)
    z = z.reshape(z.shape[0], -1)
    h = jnp.concatenate([z, dense_ctx], axis=1)
    h = jnp.maximum(h @ W_top1 + b_top1, 0.0)
    h = jnp.maximum(h @ W_top2 + b_top2, 0.0)
    y = h @ W_top3
    return y

_drawn_inputs = setup_inputs


def setup_inputs(seed=0):
    import zlib

    import numpy as np

    out = dict(_drawn_inputs(seed))
    spreads = {'b_top1': (0.0, 0.1), 'b_top2': (0.0, 0.1)}
    factors = {}
    for name, (base, spread) in spreads.items():
        noise = np.random.default_rng([zlib.crc32(name.encode()), seed]).standard_normal(out[name].shape)
        drawn = base * np.exp(spread * noise) if base else spread * noise
        out[name] = jnp.asarray(drawn.astype(out[name].dtype))
    for name, factor in factors.items():
        out[name] = (out[name] * factor).astype(out[name].dtype)
    return out
```

```python
import concourse.bass as bass
from concourse import mybir
from contextlib import ExitStack
import numpy as np

P = 128
FEATURES = 27
DIM = 128
DENSE = 16
HALVES = 2
N_ONE_HOT = 9


def feature_order(table_rows):
    smallest = sorted(range(len(table_rows)), key=lambda f: (table_rows[f], f))[:N_ONE_HOT]
    one_hot = sorted(smallest)
    return [f for f in range(len(table_rows)) if f not in one_hot], one_hot


def pair_rows(order):
    rows = []
    for j in range(1, len(order)):
        for i in range(j):
            lo, hi = min(order[i], order[j]), max(order[i], order[j])
            rows.append(hi * (hi - 1) // 2 + lo)
    return rows


def build(nc, dense, ids, ids_t, tables, w1, b1, w2, b2, w3, out):
    f32, f32r, i32 = mybir.dt.float32, mybir.dt.float32r, mybir.dt.int32
    ALU, ACT = mybir.AluOpType, mybir.ActivationFunctionType

    batch = ids.shape[0]
    MACRO = HALVES * P
    MACROS = batch // MACRO
    gathered, one_hot = feature_order([t.shape[0] for t in tables])
    NG, NO = len(gathered), len(one_hot)
    CHUNKS = 8
    ROWS_P = tables[one_hot[0]].shape[0] // CHUNKS
    HID1, HID2 = w2.shape
    SLOTS = 32
    NJ = FEATURES - 1
    QUADS = P // 4
    BANK = 512
    QB = BANK // (4 * NJ)
    GB = QUADS // QB
    PAIRS = FEATURES * NJ // 2
    K1 = PAIRS + DENSE + 1
    KC = -(-K1 // P)
    K_LAST = K1 - (KC - 1) * P
    N1, N2 = HID1 // P, HID2 // P
    XP, GP, OHR = 3, 2, 8
    TB = -(-NG // 4)
    OB = -(-NO // 2)
    UPM = 2 * TB + OB
    GPM = 2 * GB
    OPM = NO * CHUNKS
    assert UPM % XP == 0 and GPM % GP == 0 and OPM % OHR == 0 and QUADS % QB == 0

    ctx = ExitStack()
    with ctx:
        def sb(name, shape, dt=f32):
            return ctx.enter_context(nc.sbuf_tensor(name, shape, dt))

        def sem(name):
            return ctx.enter_context(nc.semaphore(name))

        ident = sb("ident", [P, P])
        row_number = sb("row_number", [P, CHUNKS])
        stage = [sb(f"stage{s}", [P, CHUNKS, DIM]) for s in range(2)]
        table_hi = [sb(f"table_hi{k}", [P, CHUNKS, DIM], f32r) for k in range(NO)]
        table_lo = [sb(f"table_lo{k}", [P, CHUNKS, DIM], f32r) for k in range(NO)]
        index = [sb(f"index{h}", [P, FEATURES], i32) for h in range(HALVES)]
        rows = [sb(f"rows{h}", [P, NG * DIM]) for h in range(HALVES)]
        id_rows = sb("id_rows", [P, NO, MACRO], i32)
        hot = [sb(f"hot{s}", [P, MACRO], f32r) for s in range(OHR)]
        emb = [sb(f"emb{h}", [P, QUADS, 4, SLOTS]) for h in range(HALVES)]
        gram = [sb(f"gram{h}", [P, NJ, QUADS]) for h in range(HALVES)]
        byj = sb("byj", [P, HALVES, NJ, SLOTS])
        feats = sb("feats", [P, HALVES, K1])
        feats_t = sb("feats_t", [P, KC, MACRO])
        w1_sb = sb("w1_sb", [P, KC, HID1])
        w2_sb = sb("w2_sb", [P, N1, HID2])
        b2_sb = sb("b2_sb", [P, N2])
        w3_sb = sb("w3_sb", [P, N2])
        h1 = sb("h1", [P, N1, MACRO])
        h2 = sb("h2", [P, N2, MACRO])
        y_row = sb("y_row", [1, MACRO])

        look = [ctx.enter_context(nc.psum_tensor(f"look{i}", [P, BANK], f32)) for i in range(XP)]
        prod = [ctx.enter_context(nc.psum_tensor(f"prod{i}", [P, BANK], f32)) for i in range(GP)]
        mlp = [ctx.enter_context(nc.psum_tensor(f"mlp{i}", [P, BANK], f32)) for i in range(3)]

        zeroed = sem("zeroed")
        consts_made = sem("consts_made")
        pads_set = sem("pads_set")
        weights_in = sem("weights_in")
        stage_in = [sem(f"stage_in{s}") for s in range(2)]
        hi_made = sem("hi_made")
        lo_made = sem("lo_made")
        index_in = [sem(f"index_in{h}") for h in range(HALVES)]
        gather_open = sem("gather_open")
        rows_in = [sem(f"rows_in{h}") for h in range(HALVES)]
        ids_in = sem("ids_in")
        hot_made = sem("hot_made")
        hot_used = sem("hot_used")
        turned_rows = sem("turned_rows")
        look_read = sem("look_read")
        prod_full = sem("prod_full")
        prod_read_a = sem("prod_read_a")
        prod_read_v = sem("prod_read_v")
        blocks_turned = sem("blocks_turned")
        pairs_packed = sem("pairs_packed")
        dense_in = sem("dense_in")
        turned_full = sem("turned_full")
        turned_read = sem("turned_read")
        l1_full, l1_read = sem("l1_full"), sem("l1_read")
        l2_full, l2_read = sem("l2_full"), sem("l2_read")
        l3_full, l3_read = sem("l3_full"), sem("l3_read")
        y_out = sem("y_out")

        N_WEIGHTS = KC + 4

        block = ctx.enter_context(nc.Block())

        def is_first(m):
            return isinstance(m, int) and m == 0

        def over_macros(engine, body):
            body(0)
            body(1)
            with engine.Fori(2, MACROS) as m:
                body(m)

        @block.sync
        def _(sp):
            def load_index(m, h):
                if not is_first(m):
                    sp.wait_ge(rows_in[h], m * (16 * NG))
                sp.dma_start(index[h][:, :], ids[bass.ds(m * MACRO + h * P, P), :]).then_inc(index_in[h], 16)

            def load_ids(m):
                if not is_first(m):
                    sp.wait_ge(hot_made, m * OPM)
                at = 0
                while at < NO:
                    n = 1
                    while at + n < NO and one_hot[at + n] == one_hot[at] + n:
                        n += 1
                    src = ids_t[one_hot[at]:one_hot[at] + n, bass.ds(m * MACRO, MACRO)]
                    sp.dma_start(id_rows[0:ROWS_P, at:at + n, :],
                                 src.rearrange("(o f) b -> o f b", o=1).broadcast_to([ROWS_P, n, MACRO])
                                 ).then_inc(ids_in, 16)
                    at += n

            def store_y(m):
                sp.wait_ge(l3_read, m + 1)
                sp.dma_start(out[bass.ds(m * MACRO, MACRO), :].rearrange("b o -> o b"),
                             y_row[0:1, :]).then_inc(y_out, 16)

            load_index(0, 0)
            load_index(0, 1)
            load_ids(0)
            for k in range(NO):
                if k >= 2:
                    sp.wait_ge(lo_made, k - 1)
                sp.dma_start(stage[k % 2][0:ROWS_P, :, :],
                             tables[one_hot[k]].rearrange("(p c) d -> p c d", c=CHUNKS)
                             ).then_inc(stage_in[k % 2], 16)
            load_ids(1)
            load_index(1, 0)
            load_index(1, 1)
            with sp.Fori(2, MACROS) as m:
                load_ids(m)
                load_index(m, 0)
                load_index(m, 1)
                store_y(m - 2)
            store_y(MACROS - 2)
            store_y(MACROS - 1)
            sp.wait_ge(y_out, 16 * MACROS)

        @block.gpsimd
        def _(pool):
            nc.gpsimd.memset(ident[:, :], 0.0).then_inc(zeroed, 1)
            nc.gpsimd.iota(row_number[:, :], pattern=[[1, CHUNKS]], base=0, channel_multiplier=CHUNKS,
                           allow_small_or_imprecise_dtypes=True).then_inc(consts_made, 1)
            pool.wait_ge(zeroed, 1)
            nc.gpsimd.affine_select(out=ident[:, :], in_=ident[:, :], compare_op=ALU.not_equal, fill=1.0,
                                    base=0, pattern=[[-1, P]], channel_multiplier=1).then_inc(consts_made, 1)

            def gather_macro(m):
                for h in range(HALVES):
                    pool.wait_ge(index_in[h], m * 16 + 16)
                    if not is_first(m):
                        pool.wait_ge(turned_rows, (m - 1) * (2 * TB) + (h + 1) * TB)
                    pool.sem_inc(gather_open, 1)
                    for g, f in enumerate(gathered):
                        nc.gpsimd.indirect_dma_start(
                            out=rows[h][:, g * DIM:(g + 1) * DIM], out_offset=None, in_=tables[f],
                            in_offset=bass.IndirectOffsetOnAxis(ap=index[h][:, f:f + 1], axis=0),
                        ).then_inc(rows_in[h], 16)

            over_macros(pool, gather_macro)

        @block.tensor
        def _(pe):
            pe.wait_ge(consts_made, 2)

            def open_look(m, u):
                if not (is_first(m) and u < XP):
                    pe.wait_ge(look_read, m * UPM + (u - XP + 1))
                return look[u % XP]

            def turn_rows(m, h, u):
                pe.wait_ge(rows_in[h], m * (16 * NG) + 16 * NG)
                for t in range(TB):
                    bank = open_look(m, u + t)
                    n = min(4, NG - 4 * t)
                    for g in range(n):
                        at = (4 * t + g) * DIM
                        last = nc.tensor.transpose(bank[:, g * P:(g + 1) * P], rows[h][:, at:at + DIM], ident[:, :])
                    last.then_inc(turned_rows, 1)

            def look_up(m, u):
                for k in range(NO):
                    if k % 2 == 0:
                        bank = open_look(m, u + k // 2)
                    if is_first(m):
                        pe.wait_ge(lo_made, k + 1)
                    dst = bank[:, (k % 2) * MACRO:(k % 2) * MACRO + MACRO]
                    for c in range(CHUNKS):
                        x = k * CHUNKS + c
                        pe.wait_ge(hot_made, m * OPM + (x + 1))
                        nc.tensor.matmul(dst, table_hi[k][0:ROWS_P, c, :], hot[x % OHR][0:ROWS_P, :],
                                         start=(c == 0), stop=False)
                        nc.tensor.matmul(dst, table_lo[k][0:ROWS_P, c, :], hot[x % OHR][0:ROWS_P, :],
                                         start=False, stop=(c == CHUNKS - 1)).then_inc(hot_used, 1)

            def products(m, h, first_bank, last_bank):
                for b in range(first_bank, last_bank):
                    g = h * GB + b
                    if not (is_first(m) and g < GP):
                        pe.wait_ge(prod_read_a, m * GPM + (g - GP + 1))
                        pe.wait_ge(prod_read_v, m * GPM + (g - GP + 1))
                    for i in range(QB):
                        q = b * QB + i
                        last = nc.tensor.matmul(prod[g % GP][:, i * 4 * NJ:(i + 1) * 4 * NJ],
                                                emb[h][:, q, :, :].rearrange("d s f -> d (s f)"),
                                                emb[h][:, q, :, 1:FEATURES],
                                                start=True, stop=True)
                    last.then_inc(prod_full, 1)

            def turn_feats(m):
                pe.wait_ge(pairs_packed, m)
                pe.wait_ge(dense_in, m * 16)
                for c in range(KC):
                    n = min(P, K1 - c * P)
                    for h in range(HALVES):
                        at = (c % 2) * MACRO + h * P
                        last = nc.tensor.transpose(mlp[c // 2][0:n, at:at + P], feats[:, h, c * P:c * P + n], ident[:, :])
                    if c % 2 == 1 or c == KC - 1:
                        last.then_inc(turned_full, 1)

            def layer1(m, first):
                if not first:
                    pe.wait_ge(l3_read, m - 1)
                pe.wait_ge(turned_read, m * 2)
                for n in range(N1):
                    bank = mlp[2] if n < 2 else mlp[0]
                    for c in range(KC):
                        k = P if c < KC - 1 else K_LAST
                        last = nc.tensor.matmul(bank[:, (n % 2) * MACRO:(n % 2 + 1) * MACRO],
                                                w1_sb[0:k, c, n * P:(n + 1) * P], feats_t[0:k, c, :],
                                                start=(c == 0), stop=(c == KC - 1))
                    if n % 2 == 1:
                        last.then_inc(l1_full, 1)

            def layer2(m):
                pe.wait_ge(l1_read, m * 2)
                for n in range(N2):
                    for c in range(N1):
                        last = nc.tensor.matmul(mlp[1][:, n * MACRO:(n + 1) * MACRO],
                                                w2_sb[:, c, n * P:(n + 1) * P], h1[:, c, :],
                                                start=(c == 0), stop=(c == N1 - 1))
                last.then_inc(l2_full, 1)

            def layer3(m):
                pe.wait_ge(l2_read, m)
                for c in range(N2):
                    last = nc.tensor.matmul(mlp[2][0:1, 0:MACRO], w3_sb[:, c:c + 1], h2[:, c, :],
                                            start=(c == 0), stop=(c == N2 - 1))
                last.then_inc(l3_full, 1)

            def macro(m):
                first = is_first(m)
                if first:
                    look_up(m, 0)
                    turn_rows(m, 0, OB)
                else:
                    turn_rows(m, 0, 0)
                    look_up(m, TB)
                    turn_feats(m)
                turn_rows(m, 1, TB + OB)
                if first:
                    pe.wait_ge(pads_set, 2)
                pe.wait_ge(look_read, m * UPM + TB + OB)
                products(m, 0, 0, GB)
                if not first:
                    if isinstance(m, int):
                        pe.wait_ge(weights_in, 16 * N_WEIGHTS)
                    layer1(m, isinstance(m, int))
                pe.wait_ge(look_read, m * UPM + UPM)
                products(m, 1, 0, GB // 2)
                if not first:
                    layer2(m)
                products(m, 1, GB // 2, GB)
                if not first:
                    layer3(m)

            over_macros(pe, macro)
            turn_feats(MACROS)
            layer1(MACROS, False)
            layer2(MACROS)
            layer3(MACROS)

        def block_of(g, s):
            return prod[g % GP][32 * s:32 * s + 32, 0:QB * 4 * NJ].rearrange(
                "p (q s j) -> p q s j", q=QB, s=4)[:, :, s, :]

        def block_to(h, b, s):
            return gram[h][32 * s:32 * s + 32, :, b * QB:(b + 1) * QB].rearrange("p j q -> p q j")

        @block.scalar
        def _(act):
            for c in range(KC):
                n = P if c < KC - 1 else K_LAST - 1
                act.dma_start(w1_sb[0:n, c, :], w1[c * P:c * P + n, :]).then_inc(weights_in, 16)
            act.dma_start(w1_sb[K_LAST - 1:K_LAST, KC - 1, :], b1).then_inc(weights_in, 16)
            act.dma_start(w2_sb[:, :, :], w2.rearrange("(c p) n -> p c n", p=P)).then_inc(weights_in, 16)
            act.dma_start(b2_sb[:, :], b2).then_inc(weights_in, 16)
            act.dma_start(w3_sb[:, :], w3).then_inc(weights_in, 16)

            def load_dense(m):
                if not is_first(m):
                    act.wait_ge(turned_full, m * 2)
                act.dma_start(feats[:, :, PAIRS:PAIRS + DENSE],
                              dense[bass.ds(m * MACRO, MACRO), :].rearrange("(h p) e -> p h e", p=P)
                              ).then_inc(dense_in, 16)

            load_dense(0)
            for k in range(NO):
                act.wait_ge(stage_in[k % 2], 16 * (k // 2 + 1))
                nc.scalar.copy(table_hi[k][0:ROWS_P, :, :], stage[k % 2][0:ROWS_P, :, :]).then_inc(hi_made, 1)

            def copy_turned(m, h, u):
                if not is_first(m):
                    act.wait_ge(prod_full, (m - 1) * GPM + (h + 1) * GB)
                for t in range(TB):
                    n = min(4, NG - 4 * t)
                    act.wait_ge(turned_rows, m * (2 * TB) + (h * TB + t + 1))
                    nc.scalar.copy(emb[h][:, :, :, 4 * t:4 * t + n].rearrange("p q s f -> p f s q"),
                                   look[(u + t) % XP][:, 0:n * P].rearrange("p (f s q) -> p f s q", s=4, q=QUADS)
                                   ).then_inc(look_read, 1)

            def pack(j):
                at = j * (j - 1) // 2
                return nc.scalar.copy(feats[:, :, at:at + j], byj[:, :, j - 1, 0:j])

            def pack_some(m, first, last):
                for j in range(first, last):
                    if j == 1:
                        act.wait_ge(blocks_turned, m * 2)
                        if not (isinstance(m, int) and m == 1):
                            act.wait_ge(turned_full, (m - 1) * 2)
                    done = pack(j)
                    if j == NJ:
                        done.then_inc(pairs_packed, 1)

            def copy_looked_up(m, u):
                if not is_first(m):
                    act.wait_ge(prod_full, m * GPM)
                for o in range(OB):
                    if not is_first(m):
                        per = -(-NJ // OB)
                        pack_some(m, 1 + o * per, min(1 + (o + 1) * per, NJ + 1))
                    n = min(2, NO - 2 * o)
                    act.wait_ge(hot_used, m * OPM + (2 * o + n) * CHUNKS)
                    at = NG + 2 * o
                    src = look[(u + o) % XP][:, 0:n * MACRO].rearrange("p (f h s q) -> p f h s q", f=n, h=HALVES, s=4)
                    for h in range(HALVES):
                        done = nc.scalar.copy(emb[h][:, :, :, at:at + n].rearrange("p q s f -> p f s q"), src[:, :, h, :, :])
                    done.then_inc(look_read, 1)

            def copy_blocks(m, h, first_bank, last_bank):
                if first_bank == 0 and not is_first(m):
                    act.wait_ge(blocks_turned, m * 2 + (h - 1))
                for b in range(first_bank, last_bank):
                    act.wait_ge(prod_full, m * GPM + (h * GB + b + 1))
                    nc.scalar.copy(block_to(h, b, 0), block_of(h * GB + b, 0))
                    nc.scalar.copy(block_to(h, b, 1), block_of(h * GB + b, 1)).then_inc(prod_read_a, 1)

            def relu1(m):
                for i in range(2):
                    act.wait_ge(l1_full, m * 2 + (i - 1))
                    nc.scalar.activation(h1[:, 2 * i:2 * i + 2, :].rearrange("p n b -> p (n b)"),
                                         mlp[2 if i == 0 else 0][:, :], ACT.Relu).then_inc(l1_read, 1)

            def relu2(m):
                act.wait_ge(l2_full, m)
                for n in range(N2):
                    done = nc.scalar.activation(h2[:, n, :], mlp[1][:, n * MACRO:(n + 1) * MACRO], ACT.Relu,
                                                bias=b2_sb[:, n:n + 1])
                done.then_inc(l2_read, 1)

            def macro(m):
                first = is_first(m)
                if first:
                    copy_looked_up(m, 0)
                    copy_turned(m, 0, OB)
                else:
                    copy_turned(m, 0, 0)
                    copy_looked_up(m, TB)
                copy_turned(m, 1, TB + OB)
                copy_blocks(m, 0, 0, GB)
                if not first:
                    load_dense(m)
                    if isinstance(m, int):
                        act.wait_ge(weights_in, 16 * N_WEIGHTS)
                    relu1(m)
                copy_blocks(m, 1, 0, GB // 2)
                if not first:
                    relu2(m)
                copy_blocks(m, 1, GB // 2, GB)

            over_macros(act, macro)
            pack_some(MACROS, 1, NJ + 1)
            relu1(MACROS)
            relu2(MACROS)

        @block.vector
        def _(dve):
            nc.vector.memset(emb[0][:, :, :, FEATURES:SLOTS], 0.0)
            nc.vector.memset(emb[1][:, :, :, FEATURES:SLOTS], 0.0).then_inc(pads_set, 1)
            nc.vector.memset(feats[:, :, K1 - 1:K1], 1.0).then_inc(pads_set, 1)
            dve.wait_ge(consts_made, 2)

            def id_loads():
                return sum(1 for k in range(NO) if k == 0 or one_hot[k] != one_hot[k - 1] + 1)

            def make_hot(m):
                dve.wait_ge(ids_in, m * (16 * id_loads()) + 16 * id_loads())
                for k in range(NO):
                    if is_first(m):
                        dve.wait_ge(hi_made, k + 1)
                        nc.vector.tensor_tensor(table_lo[k][0:ROWS_P, :, :], stage[k % 2][0:ROWS_P, :, :],
                                                table_hi[k][0:ROWS_P, :, :].bitcast(f32),
                                                ALU.subtract).then_inc(lo_made, 1)
                    for c in range(CHUNKS):
                        x = k * CHUNKS + c
                        if not (is_first(m) and x < OHR):
                            dve.wait_ge(hot_used, m * OPM + (x - OHR + 1))
                        nc.vector.tensor_scalar(hot[x % OHR][0:ROWS_P, :], id_rows[0:ROWS_P, k, :],
                                                row_number[0:ROWS_P, c:c + 1], None,
                                                ALU.is_equal).then_inc(hot_made, 1)

            def copy_feats_t(m):
                dve.wait_ge(turned_full, m * 2 - 1)
                nc.vector.tensor_copy(feats_t[:, 0:2, :].rearrange("p c b -> p (c b)"), mlp[0][:, :]).then_inc(turned_read, 1)
                dve.wait_ge(turned_full, m * 2)
                nc.vector.tensor_copy(feats_t[0:K_LAST, 2, :], mlp[1][0:K_LAST, 0:MACRO]).then_inc(turned_read, 1)

            def copy_blocks(m, h):
                for b in range(GB):
                    dve.wait_ge(prod_full, m * GPM + (h * GB + b + 1))
                    nc.vector.tensor_copy(block_to(h, b, 2), block_of(h * GB + b, 2))
                    nc.vector.tensor_copy(block_to(h, b, 3), block_of(h * GB + b, 3)).then_inc(prod_read_v, 1)

            def turn_blocks(m, h):
                dve.wait_ge(prod_read_a, m * GPM + (h + 1) * GB)
                dve.wait_ge(prod_read_v, m * GPM + (h + 1) * GB)
                if h == 0 and not is_first(m):
                    dve.wait_ge(pairs_packed, m)
                nc.vector.transpose(byj[:, h, :, :].rearrange("p j i -> p (j i)"),
                                    gram[h][:, :, :].rearrange("p j q -> p (j q)")).then_inc(blocks_turned, 1)

            def copy_y(m, first):
                if not first:
                    dve.wait_ge(y_out, (m - 1) * 16)
                dve.wait_ge(l3_full, m)
                nc.vector.tensor_copy(y_row[0:1, :], mlp[2][0:1, 0:MACRO]).then_inc(l3_read, 1)

            def macro(m):
                make_hot(m)
                if not is_first(m):
                    copy_feats_t(m)
                copy_blocks(m, 0)
                turn_blocks(m, 0)
                copy_blocks(m, 1)
                turn_blocks(m, 1)
                if not is_first(m):
                    copy_y(m, isinstance(m, int))

            over_macros(dve, macro)
            copy_feats_t(MACROS)
            copy_y(MACROS, False)


def kernel(**inputs):
    import concourse.bacc as bacc
    from concourse.bass_utils import run_bass_kernel_spmd

    nc = bacc.Bacc("TRN2", target_bir_lowering=False, num_devices=1)
    arrays = {}

    def give(name, array):
        array = np.ascontiguousarray(array)
        arrays[f"in_{name}"] = array
        return nc.dram_tensor(f"in_{name}", array.shape, mybir.dt.from_np(array.dtype), kind="ExternalInput").ap()

    tables = [np.asarray(inputs[f"tbl_{f}"]) for f in range(FEATURES)]
    gathered, one_hot = feature_order([t.shape[0] for t in tables])
    w1 = np.asarray(inputs["W_top1"])
    pairs = FEATURES * (FEATURES - 1) // 2
    rows = pair_rows(gathered + one_hot) + list(range(pairs, w1.shape[0]))
    ids = np.asarray(inputs["ids"])
    out = nc.dram_tensor("out_0", (ids.shape[0], 1), mybir.dt.float32, kind="ExternalOutput").ap()
    build(nc, give("dense", inputs["dense_ctx"]), give("ids", ids), give("ids_t", ids.T),
          [give(f"tbl_{f}", t) for f, t in enumerate(tables)],
          give("w1", w1[rows]), give("b1", np.asarray(inputs["b_top1"]).reshape(1, -1)),
          give("w2", inputs["W_top2"]), give("b2", np.asarray(inputs["b_top2"]).reshape(-1, P).T),
          give("w3", np.asarray(inputs["W_top3"]).reshape(-1, P).T), out)
    return run_bass_kernel_spmd(nc, [arrays], core_ids=[0]).results[0]["out_0"]
```

```python
import concourse.bass as bass
from concourse import mybir
from contextlib import ExitStack
import numpy as np

P = 128
FEATURES = 27
DIM = 128
DENSE = 16
HALVES = 2
MACRO = HALVES * P
N_ONE_HOT = 8


def feature_order(table_rows):
    smallest = sorted(range(len(table_rows)), key=lambda f: (table_rows[f], f))[:N_ONE_HOT]
    one_hot = sorted(smallest)
    return [f for f in range(len(table_rows)) if f not in one_hot], one_hot


def pair_rows(order):
    rows = []
    for j in range(1, len(order)):
        for i in range(j):
            lo, hi = min(order[i], order[j]), max(order[i], order[j])
            rows.append(hi * (hi - 1) // 2 + lo)
    return rows


def build(nc, dense, ids, ids_t, tables, w1, b1, w2, b2, w3, out):
    f32, f32r, i32 = mybir.dt.float32, mybir.dt.float32r, mybir.dt.int32
    ALU, ACT = mybir.AluOpType, mybir.ActivationFunctionType

    batch = ids.shape[0]
    MACROS = batch // MACRO
    gathered, one_hot = feature_order([t.shape[0] for t in tables])
    NG, NO = len(gathered), len(one_hot)
    CHUNKS = 8
    ROWS_P = tables[one_hot[0]].shape[0] // CHUNKS
    HID1, HID2 = w2.shape
    NI = FEATURES - 1
    BLOCK = 32
    NJ = FEATURES - 1
    QUADS = P // 4
    BANK = 512
    QB = BANK // (4 * NJ)
    GB = QUADS // QB
    PAIRS = FEATURES * NJ // 2
    K1 = PAIRS + DENSE + 1
    KC = -(-K1 // P)
    K_LAST = K1 - (KC - 1) * P
    N1, N2 = HID1 // P, HID2 // P
    XP, GP, OHR = 4, 2, 8
    TB = -(-NG // 4)
    UPM = 2 * TB + NO
    GPM = 2 * GB
    GROUPS = [(k, min(2, NO - k)) for k in range(0, NO, 2)]
    STEPS = [(k, n, c) for k, n in GROUPS for c in range(CHUNKS)]
    OPM = len(STEPS)
    PACK_GROUPS = max(1, len(GROUPS) - 2)
    EARLY = GROUPS[-1][0]
    AT_ROWS = [EARLY, NO + TB]
    HEAD = 2 * OHR
    STAGES = 4
    assert GPM % GP == 0 and OPM % OHR == 0 and QUADS % QB == 0 and QUADS == BLOCK

    ctx = ExitStack()
    with ctx:
        def sb(name, shape, dt=f32):
            return ctx.enter_context(nc.sbuf_tensor(name, shape, dt))

        def sem(name):
            return ctx.enter_context(nc.semaphore(name))

        ident = sb("ident", [P, P])
        first_row = sb("first_row", [P, 1])
        table_hi = [sb(f"table_hi{k}", [P, CHUNKS, DIM], f32r) for k in range(NO)]
        table_lo = [sb(f"table_lo{k}", [P, CHUNKS, DIM], f32r) for k in range(NO)]
        index = [sb(f"index{h}", [P, FEATURES], i32) for h in range(HALVES)]
        rows = [sb(f"rows{h}", [P, NG * DIM]) for h in range(HALVES)]
        id_rows = sb("id_rows", [P, NO, MACRO], i32)
        id_steps = sb("id_steps", [P, NO, MACRO])
        hot = [sb(f"hot{s}", [P, 2, MACRO], f32r) for s in range(OHR)]
        emb = [sb(f"emb{h}", [P, QUADS, 4, FEATURES]) for h in range(HALVES)]
        wide = sb("wide", [P, 4, NJ, QUADS])
        gram = sb("gram", [P, NJ, QUADS])
        byj = sb("byj", [P, HALVES, NJ, BLOCK])
        free = [wide[:, :, :, :].rearrange("p s j q -> p (s j q)")[:, i * CHUNKS * DIM:(i + 1) * CHUNKS * DIM]
                for i in range(STAGES - 1)]
        free += [byj[:, :, :, :].rearrange("p h j i -> p (h j i)")[:, 0:CHUNKS * DIM]]
        stage = [f.rearrange("p (c d) -> p c d", c=CHUNKS) for f in free]
        feats = sb("feats", [P, HALVES, K1])
        feats_t = sb("feats_t", [P, KC, MACRO])
        w1_sb = sb("w1_sb", [P, KC, HID1])
        w2_sb = sb("w2_sb", [P, N1, HID2])
        b2_sb = sb("b2_sb", [P, N2])
        w3_sb = sb("w3_sb", [P, N2])
        h1 = sb("h1", [P, N1, MACRO])
        h2 = sb("h2", [P, N2, MACRO])
        y_row = sb("y_row", [1, MACRO])

        look = [ctx.enter_context(nc.psum_tensor(f"look{i}", [P, BANK], f32)) for i in range(XP)]
        prod = [ctx.enter_context(nc.psum_tensor(f"prod{i}", [P, BANK], f32)) for i in range(GP)]
        mlp = [ctx.enter_context(nc.psum_tensor(f"mlp{i}", [P, BANK], f32)) for i in range(2)]

        zeroed = sem("zeroed")
        consts_made = sem("consts_made")
        pads_set = sem("pads_set")
        weights_in = sem("weights_in")
        stage_in = [sem(f"stage_in{s}") for s in range(STAGES)]
        hi_made = sem("hi_made")
        lo_made = sem("lo_made")
        index_in = [sem(f"index_in{h}") for h in range(HALVES)]
        gather_open = sem("gather_open")
        rows_in = [sem(f"rows_in{h}") for h in range(HALVES)]
        ids_in = sem("ids_in")
        steps_made = sem("steps_made")
        hot_made = sem("hot_made")
        hot_used = sem("hot_used")
        turned_rows = sem("turned_rows")
        look_read = sem("look_read")
        prod_full = sem("prod_full")
        prod_read = sem("prod_read")
        blocks_in = sem("blocks_in")
        blocks_turned = sem("blocks_turned")
        pairs_packed = sem("pairs_packed")
        dense_in = sem("dense_in")
        turned_full = sem("turned_full")
        turned_read = sem("turned_read")
        l1_full, l1_read = sem("l1_full"), sem("l1_read")
        l2_full, l2_read = sem("l2_full"), sem("l2_read")
        l3_full, l3_read = sem("l3_full"), sem("l3_read")
        y_out = sem("y_out")

        N_WEIGHTS = KC + 4

        block = ctx.enter_context(nc.Block())

        def is_first(m):
            return isinstance(m, int) and m == 0

        def look_bank(k):
            return k if k < EARLY else k + TB

        def is_last(m):
            return isinstance(m, int) and m == MACROS - 1

        def over_macros(engine, body):
            body(0)
            body(1)
            with engine.Fori(2, MACROS - 1) as m:
                body(m)
            body(MACROS - 1)

        @block.sync
        def _(sp):
            def load_index(m, h):
                if not is_first(m):
                    sp.wait_ge(rows_in[h], m * (16 * NG))
                sp.dma_start(index[h][:, :], ids[bass.ds(m * MACRO + h * P, P), :]).then_inc(index_in[h], 16)

            def load_ids(m):
                if not is_first(m):
                    sp.wait_ge(steps_made, m)
                src = ids_t[bass.ds(m, 1), :, :]
                sp.dma_start(id_rows[0:ROWS_P, :, :], src.broadcast_to([ROWS_P, NO, MACRO])).then_inc(ids_in, 16)

            def load_stage(k):
                if k >= STAGES:
                    sp.wait_ge(lo_made, k - STAGES + 1)
                sp.dma_start(stage[k % STAGES][0:ROWS_P, :, :],
                             tables[one_hot[k]].rearrange("(p c) d -> p c d", c=CHUNKS)
                             ).then_inc(stage_in[k % STAGES], 16)

            def load_weights():
                for c in range(KC):
                    n = P if c < KC - 1 else K_LAST - 1
                    sp.dma_start(w1_sb[0:n, c, :], w1[c * P:c * P + n, :]).then_inc(weights_in, 16)
                sp.dma_start(w1_sb[K_LAST - 1:K_LAST, KC - 1, :], b1).then_inc(weights_in, 16)
                sp.dma_start(w2_sb[:, :, :], w2.rearrange("(c p) n -> p c n", p=P)).then_inc(weights_in, 16)
                sp.dma_start(b2_sb[:, :], b2).then_inc(weights_in, 16)
                sp.dma_start(w3_sb[:, :], w3).then_inc(weights_in, 16)

            def move_blocks(m, h):
                sp.wait_ge(prod_read, m * GPM + (h + 1) * GB)
                for s in range(4):
                    sp.dma_start(gram[BLOCK * s:BLOCK * s + NI, :, :].rearrange("p j q -> p (j q)"),
                                 wide[FEATURES * s:FEATURES * s + NI, s, :, :].rearrange("p j q -> p (j q)")
                                 ).then_inc(blocks_in, 16)

            def store_y(m):
                sp.wait_ge(l3_read, m + 1)
                sp.dma_start(out[bass.ds(m * MACRO, MACRO), :].rearrange("b o -> o b"),
                             y_row[0:1, :]).then_inc(y_out, 16)

            def macro(m, last=False):
                if not last:
                    load_index(m + 1, 0)
                    load_ids(m + 1)
                    load_index(m + 1, 1)
                if is_first(m):
                    sp.wait_ge(pads_set, 2)
                move_blocks(m, 0)
                if not last:
                    if not is_first(m):
                        store_y(m - 1)
                    move_blocks(m, 1)

            load_index(0, 0)
            load_stage(0)
            load_ids(0)
            load_stage(1)
            load_index(0, 1)
            for k in range(2, NO):
                load_stage(k)
            load_weights()
            for m in range(2):
                macro(m)
            with sp.Fori(2, MACROS - 1) as m:
                macro(m)
            macro(MACROS - 1, last=True)
            move_blocks(MACROS - 1, 1)
            store_y(MACROS - 2)
            store_y(MACROS - 1)
            sp.wait_ge(y_out, 16 * MACROS)

        @block.gpsimd
        def _(pool):
            nc.gpsimd.memset(ident[:, :], 0.0).then_inc(zeroed, 1)
            nc.gpsimd.iota(first_row[:, :], pattern=[[0, 1]], base=0, channel_multiplier=CHUNKS,
                           allow_small_or_imprecise_dtypes=True).then_inc(consts_made, 1)
            pool.wait_ge(zeroed, 1)
            nc.gpsimd.affine_select(out=ident[:, :], in_=ident[:, :], compare_op=ALU.not_equal, fill=1.0,
                                    base=0, pattern=[[-1, P]], channel_multiplier=1).then_inc(consts_made, 1)

            def gather_macro(m):
                for h in range(HALVES):
                    pool.wait_ge(index_in[h], m * 16 + 16)
                    if not is_first(m):
                        pool.wait_ge(turned_rows, (m - 1) * (2 * TB) + (h + 1) * TB)
                    pool.sem_inc(gather_open, 1)
                    for g, f in enumerate(gathered):
                        nc.gpsimd.indirect_dma_start(
                            out=rows[h][:, g * DIM:(g + 1) * DIM], out_offset=None, in_=tables[f],
                            in_offset=bass.IndirectOffsetOnAxis(ap=index[h][:, f:f + 1], axis=0),
                        ).then_inc(rows_in[h], 16)

            over_macros(pool, gather_macro)

        @block.tensor
        def _(pe):
            pe.wait_ge(consts_made, 2)

            def open_look(m, u):
                before = u - XP if u >= XP else max(x for x in range(UPM) if x % XP == u) - UPM
                if not (is_first(m) and before < 0):
                    pe.wait_ge(look_read, m * UPM + (before + 1))
                return look[u % XP]

            def turn_rows(m, h, u):
                pe.wait_ge(rows_in[h], m * (16 * NG) + 16 * NG)
                for t in range(TB):
                    bank = open_look(m, u + t)
                    n = min(4, NG - 4 * t)
                    for g in range(n):
                        at = (4 * t + g) * DIM
                        last = nc.tensor.transpose(bank[:, g * P:(g + 1) * P], rows[h][:, at:at + DIM], ident[:, :])
                    last.then_inc(turned_rows, 1)

            def look_up(m, first_table, last_table):
                for x, (k, n, c) in enumerate(STEPS):
                    if not first_table <= k < last_table:
                        continue
                    if c == 0:
                        bank = [open_look(m, look_bank(k + i)) for i in range(n)]
                        if is_first(m):
                            pe.wait_ge(lo_made, k + n)
                    pe.wait_ge(hot_made, m * OPM + (x + 1))
                    for i in range(n):
                        seen = hot[x % OHR][0:ROWS_P, i, :]
                        nc.tensor.matmul(bank[i][:, 0:MACRO], table_hi[k + i][0:ROWS_P, c, :], seen,
                                         start=(c == 0), stop=False)
                        last = nc.tensor.matmul(bank[i][:, 0:MACRO], table_lo[k + i][0:ROWS_P, c, :], seen,
                                                start=False, stop=(c == CHUNKS - 1))
                    last.then_inc(hot_used, 1)

            def products(m, h, first_bank, last_bank):
                for b in range(first_bank, last_bank):
                    g = h * GB + b
                    if not (is_first(m) and g < GP):
                        pe.wait_ge(prod_read, m * GPM + (g - GP + 1))
                    for i in range(QB):
                        q = b * QB + i
                        last = nc.tensor.matmul(prod[g % GP][0:4 * FEATURES, i * 4 * NJ:(i + 1) * 4 * NJ],
                                                emb[h][:, q, :, :].rearrange("d s f -> d (s f)"),
                                                emb[h][:, q, :, 1:FEATURES],
                                                start=True, stop=True)
                    last.then_inc(prod_full, 1)

            def turn_feats(m):
                pe.wait_ge(pairs_packed, m)
                pe.wait_ge(dense_in, m * 16)
                for c in range(KC):
                    if c == 2 and not (isinstance(m, int) and m == 1):
                        pe.wait_ge(l3_read, m - 1)
                    n = min(P, K1 - c * P)
                    for h in range(HALVES):
                        at = (c % 2) * MACRO + h * P
                        last = nc.tensor.transpose(mlp[c // 2][0:n, at:at + P], feats[:, h, c * P:c * P + n], ident[:, :])
                    if c % 2 == 1 or c == KC - 1:
                        last.then_inc(turned_full, 1)

            def layer1(m, first_n, last_n):
                pe.wait_ge(turned_read, m * 2)
                for n in range(first_n, last_n):
                    bank = mlp[n // 2]
                    for c in range(KC):
                        k = P if c < KC - 1 else K_LAST
                        last = nc.tensor.matmul(bank[:, (n % 2) * MACRO:(n % 2 + 1) * MACRO],
                                                w1_sb[0:k, c, n * P:(n + 1) * P], feats_t[0:k, c, :],
                                                start=(c == 0), stop=(c == KC - 1))
                    if n % 2 == 1:
                        last.then_inc(l1_full, 1)

            def layer2(m):
                pe.wait_ge(l1_read, m * 2)
                for n in range(N2):
                    for c in range(N1):
                        last = nc.tensor.matmul(mlp[0][:, n * MACRO:(n + 1) * MACRO],
                                                w2_sb[:, c, n * P:(n + 1) * P], h1[:, c, :],
                                                start=(c == 0), stop=(c == N1 - 1))
                last.then_inc(l2_full, 1)

            def layer3(m):
                pe.wait_ge(l2_read, m)
                for c in range(N2):
                    last = nc.tensor.matmul(mlp[1][0:1, 0:MACRO], w3_sb[:, c:c + 1], h2[:, c, :],
                                            start=(c == 0), stop=(c == N2 - 1))
                last.then_inc(l3_full, 1)

            def macro(m):
                first = is_first(m)
                look_up(m, 0, EARLY)
                turn_rows(m, 0, AT_ROWS[0])
                look_up(m, EARLY, NO)
                if not first:
                    turn_feats(m)
                pe.wait_ge(look_read, m * UPM + NO + TB)
                products(m, 0, 0, GB)
                if not first:
                    if isinstance(m, int):
                        pe.wait_ge(weights_in, 16 * N_WEIGHTS)
                    if not is_last(m):
                        layer1(m, 0, N1)
                turn_rows(m, 1, AT_ROWS[1])
                if is_last(m):
                    layer1(m, 0, N1 // 2)
                elif not first:
                    layer2(m)
                pe.wait_ge(look_read, m * UPM + UPM)
                products(m, 1, 0, GB // 2)
                if not first and not is_last(m):
                    layer3(m)
                products(m, 1, GB // 2, GB)
                if is_last(m):
                    layer1(m, N1 // 2, N1)
                    layer2(m)
                    layer3(m)

            over_macros(pe, macro)
            turn_feats(MACROS)
            layer1(MACROS, 0, N1)
            layer2(MACROS)
            layer3(MACROS)

        @block.scalar
        def _(act):
            def load_dense(m):
                if not is_first(m):
                    act.wait_ge(turned_full, m * 2)
                act.dma_start(feats[:, :, PAIRS:PAIRS + DENSE],
                              dense[bass.ds(m * MACRO, MACRO), :].rearrange("(h p) e -> p h e", p=P)
                              ).then_inc(dense_in, 16)

            load_dense(0)

            def round_tables(k, n):
                for t in range(k, k + n):
                    act.wait_ge(stage_in[t % STAGES], 16 * (t // STAGES + 1))
                    nc.scalar.copy(table_hi[t][0:ROWS_P, :, :], stage[t % STAGES][0:ROWS_P, :, :]).then_inc(hi_made, 1)

            def copy_turned(m, h, u):
                if not is_first(m):
                    act.wait_ge(prod_full, (m - 1) * GPM + (h + 1) * GB)
                for t in range(TB):
                    n = min(4, NG - 4 * t)
                    act.wait_ge(turned_rows, m * (2 * TB) + (h * TB + t + 1))
                    nc.scalar.copy(emb[h][:, :, :, 4 * t:4 * t + n].rearrange("p q s f -> p f s q"),
                                   look[(u + t) % XP][:, 0:n * P].rearrange("p (f s q) -> p f s q", s=4, q=QUADS)
                                   ).then_inc(look_read, 1)

            def pack(j):
                at = j * (j - 1) // 2
                return nc.scalar.copy(feats[:, :, at:at + j], byj[:, :, j - 1, 0:j])

            def pack_some(m, first, last):
                for j in range(first, last):
                    if j == 1:
                        act.wait_ge(blocks_turned, m * 2)
                        if not (isinstance(m, int) and m == 1):
                            act.wait_ge(turned_full, (m - 1) * 2)
                    done = pack(j)
                    if j == NJ:
                        done.then_inc(pairs_packed, 1)

            def copy_looked_up(m, first_group, last_group):
                if first_group == 0:
                    if is_first(m):
                        round_tables(*GROUPS[0])
                    else:
                        act.wait_ge(prod_full, m * GPM)
                for g in range(first_group, last_group):
                    k, n = GROUPS[g]
                    if is_first(m) and g + 1 < len(GROUPS):
                        round_tables(*GROUPS[g + 1])
                    act.wait_ge(hot_used, m * OPM + (g + 1) * CHUNKS)
                    for i in range(n):
                        bank = look[look_bank(k + i) % XP]
                        src = bank[:, 0:MACRO].rearrange("p (h s q) -> p h s q", h=HALVES, s=4)
                        for h in range(HALVES):
                            done = nc.scalar.copy(emb[h][:, :, :, NG + k + i].rearrange("p q s -> p s q"), src[:, h, :, :])
                        done.then_inc(look_read, 1)
                    if not is_first(m) and g < PACK_GROUPS:
                        per = -(-NJ // PACK_GROUPS)
                        pack_some(m, 1 + g * per, min(1 + (g + 1) * per, NJ + 1))

            def copy_products(m, h, first_bank, last_bank):
                if first_bank == 0 and not (is_first(m) and h == 0):
                    act.wait_ge(blocks_in, m * (2 * 64) + h * 64)
                for b in range(first_bank, last_bank):
                    g = h * GB + b
                    if b == GB - 1 and not (is_first(m) and h == 0):
                        act.wait_ge(blocks_turned, m * 2 + h)
                    act.wait_ge(prod_full, m * GPM + (g + 1))
                    nc.scalar.copy(wide[0:4 * FEATURES, :, :, b * QB:(b + 1) * QB].rearrange("p s j q -> p q s j"),
                                   prod[g % GP][0:4 * FEATURES, 0:QB * 4 * NJ].rearrange(
                                       "p (q s j) -> p q s j", q=QB, s=4)).then_inc(prod_read, 1)

            def relu1(m, first_bank, last_bank):
                for i in range(first_bank, last_bank):
                    act.wait_ge(l1_full, m * 2 + (i - 1))
                    nc.scalar.activation(h1[:, 2 * i:2 * i + 2, :].rearrange("p n b -> p (n b)"),
                                         mlp[i][:, :], ACT.Relu).then_inc(l1_read, 1)

            def relu2(m):
                act.wait_ge(l2_full, m)
                for n in range(N2):
                    done = nc.scalar.activation(h2[:, n, :], mlp[0][:, n * MACRO:(n + 1) * MACRO], ACT.Relu,
                                                bias=b2_sb[:, n:n + 1])
                done.then_inc(l2_read, 1)

            def macro(m):
                first = is_first(m)
                copy_looked_up(m, 0, len(GROUPS) - 1)
                copy_turned(m, 0, AT_ROWS[0])
                copy_looked_up(m, len(GROUPS) - 1, len(GROUPS))
                copy_products(m, 0, 0, GB)
                if not first:
                    load_dense(m)
                    if not is_last(m):
                        relu1(m, 0, 2)
                copy_turned(m, 1, AT_ROWS[1])
                if is_last(m):
                    relu1(m, 0, 1)
                elif not first:
                    if isinstance(m, int):
                        act.wait_ge(weights_in, 16 * N_WEIGHTS)
                    relu2(m)
                copy_products(m, 1, 0, GB)
                if is_last(m):
                    relu1(m, 1, 2)

            over_macros(act, macro)
            pack_some(MACROS, 1, NJ + 1)
            relu2(MACROS - 1)
            relu1(MACROS, 0, 2)
            relu2(MACROS)

        @block.vector
        def _(dve):
            nc.vector.memset(gram[:, :, :], 0.0).then_inc(pads_set, 1)
            nc.vector.memset(feats[:, :, K1 - 1:K1], 1.0).then_inc(pads_set, 1)
            dve.wait_ge(consts_made, 2)

            def make_steps(m):
                dve.wait_ge(ids_in, m * 16 + 16)
                if not is_first(m):
                    dve.wait_ge(hot_made, m * OPM)
                nc.vector.tensor_scalar(id_steps[0:ROWS_P, :, :], id_rows[0:ROWS_P, :, :],
                                        first_row[0:ROWS_P, 0:1], None, ALU.subtract).then_inc(steps_made, 1)
                dve.wait_ge(steps_made, m + 1)

            def make_rest(k, n):
                for t in range(k, k + n):
                    dve.wait_ge(hi_made, t + 1)
                    nc.vector.tensor_tensor(table_lo[t][0:ROWS_P, :, :], stage[t % STAGES][0:ROWS_P, :, :],
                                            table_hi[t][0:ROWS_P, :, :].bitcast(f32),
                                            ALU.subtract).then_inc(lo_made, 1)

            def make_hot(m, first_step, last_step):
                for x in range(first_step, last_step):
                    k, n, c = STEPS[x]
                    if is_first(m) and c == 0:
                        make_rest(k, n)
                    if not (is_first(m) and x < OHR):
                        dve.wait_ge(hot_used, m * OPM + (x - OHR + 1))
                    nc.vector.tensor_scalar(hot[x % OHR][0:ROWS_P, 0:n, :], id_steps[0:ROWS_P, k:k + n, :],
                                            float(c), None, ALU.is_equal).then_inc(hot_made, 1)

            def copy_feats_t(m):
                dve.wait_ge(turned_full, m * 2 - 1)
                nc.vector.tensor_copy(feats_t[:, 0:2, :].rearrange("p c b -> p (c b)"), mlp[0][:, :]).then_inc(turned_read, 1)
                dve.wait_ge(turned_full, m * 2)
                nc.vector.tensor_copy(feats_t[0:K_LAST, 2, :], mlp[1][0:K_LAST, 0:MACRO]).then_inc(turned_read, 1)

            def turn_blocks(m, h):
                dve.wait_ge(blocks_in, m * (2 * 64) + (h + 1) * 64)
                if h == 0 and not is_first(m):
                    dve.wait_ge(pairs_packed, m)
                nc.vector.transpose(byj[:, h, :, :].rearrange("p j i -> p (j i)"),
                                    gram[:, :, :].rearrange("p j q -> p (j q)")).then_inc(blocks_turned, 1)

            def copy_y(m, first=False):
                if not first:
                    dve.wait_ge(y_out, m * 16 - 16)
                dve.wait_ge(l3_full, m)
                nc.vector.tensor_copy(y_row[0:1, :], mlp[1][0:1, 0:MACRO]).then_inc(l3_read, 1)

            def macro(m):
                make_steps(m)
                make_hot(m, 0, HEAD)
                if not is_first(m):
                    turn_blocks(m - 1, 1)
                make_hot(m, HEAD, OPM)
                if not is_first(m):
                    copy_feats_t(m)
                turn_blocks(m, 0)
                if not is_first(m) and not is_last(m):
                    copy_y(m, isinstance(m, int) and m == 1)

            over_macros(dve, macro)
            turn_blocks(MACROS - 1, 1)
            copy_y(MACROS - 1)
            copy_feats_t(MACROS)
            copy_y(MACROS)


def kernel(**inputs):
    import concourse.bacc as bacc
    from concourse.bass_utils import run_bass_kernel_spmd

    nc = bacc.Bacc("TRN2", target_bir_lowering=False, num_devices=1)
    arrays = {}

    def give(name, array):
        array = np.ascontiguousarray(array)
        arrays[f"in_{name}"] = array
        return nc.dram_tensor(f"in_{name}", array.shape, mybir.dt.from_np(array.dtype), kind="ExternalInput").ap()

    tables = [np.asarray(inputs[f"tbl_{f}"]) for f in range(FEATURES)]
    gathered, one_hot = feature_order([t.shape[0] for t in tables])
    w1 = np.asarray(inputs["W_top1"])
    pairs = FEATURES * (FEATURES - 1) // 2
    rows = pair_rows(gathered + one_hot) + list(range(pairs, w1.shape[0]))
    ids = np.asarray(inputs["ids"])
    out = nc.dram_tensor("out_0", (ids.shape[0], 1), mybir.dt.float32, kind="ExternalOutput").ap()
    build(nc, give("dense", inputs["dense_ctx"]), give("ids", ids), give("ids_t", ids[:, one_hot].reshape(-1, MACRO, len(one_hot)).transpose(0, 2, 1)),
          [give(f"tbl_{f}", t) for f, t in enumerate(tables)],
          give("w1", w1[rows]), give("b1", np.asarray(inputs["b_top1"]).reshape(1, -1)),
          give("w2", inputs["W_top2"]), give("b2", np.asarray(inputs["b_top2"]).reshape(-1, P).T),
          give("w3", np.asarray(inputs["W_top3"]).reshape(-1, P).T), out)
    return run_bass_kernel_spmd(nc, [arrays], core_ids=[0]).results[0]["out_0"]
```

```python
import concourse.bass as bass
from concourse import mybir
from contextlib import ExitStack
import numpy as np

P = 128
FEATURES = 27
DIM = 128
DENSE = 16
HALVES = 2
MACRO = HALVES * P
N_ONE_HOT = 9


def feature_order(table_rows):
    smallest = sorted(range(len(table_rows)), key=lambda f: (table_rows[f], f))[:N_ONE_HOT]
    one_hot = sorted(smallest)
    return [f for f in range(len(table_rows)) if f not in one_hot], one_hot


def pair_rows(order):
    rows = []
    for j in range(1, len(order)):
        for i in range(j):
            lo, hi = min(order[i], order[j]), max(order[i], order[j])
            rows.append(hi * (hi - 1) // 2 + lo)
    return rows


def build(nc, dense, ids, ids_t, tables, w1, b1, w2, b2, w3, out):
    f32, f32r, i32 = mybir.dt.float32, mybir.dt.float32r, mybir.dt.int32
    ALU, ACT = mybir.AluOpType, mybir.ActivationFunctionType

    batch = ids.shape[0]
    MACROS = batch // MACRO
    gathered, one_hot = feature_order([t.shape[0] for t in tables])
    NG, NO = len(gathered), len(one_hot)
    CHUNKS = 8
    ROWS_P = tables[one_hot[0]].shape[0] // CHUNKS
    HID1, HID2 = w2.shape
    NI = FEATURES - 1
    BLOCK = 32
    NJ = FEATURES - 1
    QUADS = P // 4
    BANK = 512
    BANKS = 2
    QB = QUADS // BANKS
    PAIRS = FEATURES * NJ // 2
    K1 = PAIRS + DENSE + 1
    KC = -(-K1 // P)
    K_LAST = K1 - (KC - 1) * P
    N1, N2 = HID1 // P, HID2 // P
    XP = 4
    OHR = 8
    TB = -(-NG // 4)
    UPM = 2 * TB + NO
    GROUPS = ([(0, 1)] if NO % 2 else []) + [(k, 2) for k in range(NO % 2, NO, 2)]
    STEPS = [(k, n, c) for k, n in GROUPS for c in range(CHUNKS)]
    OPM = len(STEPS)
    AHEAD = GROUPS[1][0]
    EARLY = GROUPS[len(GROUPS) // 2][0]
    HEAD = OHR
    MIDDLE = 2 * OHR
    ACT_PACKS = 18
    STAGES = 4
    EARLY_ROWS = 4 * (TB - 1)
    ID_PARTS = [(0, GROUPS[0][1]), (GROUPS[1][0], GROUPS[2][0]), (GROUPS[2][0], NO)]
    assert N2 == 2 and OPM % OHR == 0 and QB * NJ <= BANK and QUADS == BLOCK

    ctx = ExitStack()
    with ctx:
        def sb(name, shape, dt=f32):
            return ctx.enter_context(nc.sbuf_tensor(name, shape, dt))

        def sem(name):
            return ctx.enter_context(nc.semaphore(name))

        ident = sb("ident", [P, P])
        first_row = sb("first_row", [P, 1])
        table_hi = [sb(f"table_hi{k}", [P, CHUNKS, DIM], f32r) for k in range(NO)]
        table_lo = [sb(f"table_lo{k}", [P, CHUNKS, DIM], f32r) for k in range(NO)]
        index = [sb(f"index{h}", [P, FEATURES], i32) for h in range(HALVES)]
        rows = [sb(f"rows{h}", [P, NG * DIM]) for h in range(HALVES)]
        id_rows = sb("id_rows", [P, NO, MACRO], i32)
        id_steps = sb("id_steps", [P, NO, MACRO])
        hot = [sb(f"hot{s}", [P, 2, MACRO], f32r) for s in range(OHR)]
        waiting = sb("waiting", [P, NO, P])
        emb = [sb(f"emb{h}", [P, QUADS, 4, FEATURES]) for h in range(HALVES)]
        byj = sb("byj", [P, HALVES, NJ, BLOCK])
        free = [emb[1][:, :, :, :].rearrange("p q s f -> p (q s f)")[:, i * CHUNKS * DIM:(i + 1) * CHUNKS * DIM]
                for i in range(STAGES - 1)]
        free += [byj[:, :, :, :].rearrange("p h j i -> p (h j i)")[:, 0:CHUNKS * DIM]]
        stage = [f.rearrange("p (c d) -> p c d", c=CHUNKS) for f in free]
        feats = sb("feats", [P, HALVES, K1])
        feats_t = sb("feats_t", [P, KC, MACRO])
        w1_sb = sb("w1_sb", [P, KC, HID1])
        w2_sb = sb("w2_sb", [P, N1, HID2])
        b2_sb = sb("b2_sb", [P, N2])
        w3_sb = sb("w3_sb", [P, N2])
        h1 = sb("h1", [P, N1, MACRO])
        h2 = sb("h2", [P, N2, MACRO])
        ones = sb("ones", [P, 1])
        weighed_h2 = sb("weighed_h2", [P, MACRO])
        y_row = sb("y_row", [1, MACRO])

        look = [ctx.enter_context(nc.psum_tensor(f"look{i}", [P, BANK], f32)) for i in range(XP)]
        prod = ctx.enter_context(nc.psum_tensor("prod", [P, BANKS, BANK], f32))
        mlp = [ctx.enter_context(nc.psum_tensor(f"mlp{i}", [P, BANK], f32)) for i in range(2)]

        half_banks = [[mlp[1], mlp[0], look[2]], [look[0], look[1], look[3]]]

        zeroed = sem("zeroed")
        consts_made = sem("consts_made")
        pads_set = sem("pads_set")
        weights_in = sem("weights_in")
        stage_in = [sem(f"stage_in{s}") for s in range(STAGES)]
        hi_made = sem("hi_made")
        lo_made = sem("lo_made")
        index_in = [sem(f"index_in{h}") for h in range(HALVES)]
        gather_open = sem("gather_open")
        rows_in = [sem(f"rows_in{h}") for h in range(HALVES)]
        last_rows_in = [sem(f"last_rows_in{h}") for h in range(HALVES)]
        first_ids_in = [sem(f"first_ids_in{i}") for i in range(len(ID_PARTS) - 1)]
        ids_in = sem("ids_in")
        steps_made = sem("steps_made")
        hot_made = sem("hot_made")
        hot_used = sem("hot_used")
        turned_rows = sem("turned_rows")
        look_read = sem("look_read")
        joined = sem("joined")
        prod_full = sem("prod_full")
        blocks_turned = sem("blocks_turned")
        pairs_packed = sem("pairs_packed")
        last_packed = sem("last_packed")
        dense_in = sem("dense_in")
        turned_full = sem("turned_full")
        turned_read = sem("turned_read")
        l1_full, l1_read = sem("l1_full"), sem("l1_read")
        l2_full, l2_read = sem("l2_full"), sem("l2_read")
        h2_half_weighed = sem("h2_half_weighed")
        h2_weighed = sem("h2_weighed")
        l3_full, l3_read = sem("l3_full"), sem("l3_read")
        y_out = sem("y_out")

        N_WEIGHTS = KC + 4

        block = ctx.enter_context(nc.Block())

        def is_first(m):
            return isinstance(m, int) and m == 0

        def is_last(m):
            return isinstance(m, int) and m == MACROS - 1

        def uses(m):
            return NO + m * UPM

        def rows_at(m, h):
            return 0 if h == 0 else TB if is_last(m) else TB + EARLY

        def table_at(k):
            return TB + k if k < EARLY else 2 * TB + k

        def use_before(m, v):
            if v >= XP:
                return uses(m) + (v - XP + 1)
            if is_first(m):
                return max(k for k in range(NO) if k % XP == v % XP) + 1
            return uses(m - 1) + (max(x for x in range(UPM) if x % XP == v % XP) + 1)

        def over_macros(engine, body, last_body=None):
            body(0)
            body(1)
            with engine.Fori(2, MACROS - 1) as m:
                body(m)
            (last_body or body)(MACROS - 1)

        @block.sync
        def _(sp):
            def load_index(m, h):
                if not is_first(m):
                    sp.wait_ge(turned_rows, (m - 1) * (2 * TB) + (h + 1) * TB)
                sp.dma_start(index[h][:, :], ids[bass.ds(m * MACRO + h * P, P), :]).then_inc(index_in[h], 16)

            def load_first_ids(i):
                first, last = ID_PARTS[i]
                sp.dma_start(id_rows[0:ROWS_P, first:last, :],
                             ids_t[0:1, first:last, :].broadcast_to([ROWS_P, last - first, MACRO])).then_inc(
                                 first_ids_in[i] if i < len(ID_PARTS) - 1 else ids_in, 16)

            def load_ids(m):
                sp.wait_ge(steps_made, m + (len(ID_PARTS) - 1))
                sp.dma_start(id_rows[0:ROWS_P, :, :],
                             ids_t[bass.ds(m, 1), :, :].broadcast_to([ROWS_P, NO, MACRO])).then_inc(ids_in, 16)

            def load_stage(k):
                if k >= STAGES:
                    sp.wait_ge(lo_made, k - STAGES + 1)
                sp.dma_start(stage[k % STAGES][0:ROWS_P, :, :],
                             tables[one_hot[k]].rearrange("(p c) d -> p c d", c=CHUNKS)
                             ).then_inc(stage_in[k % STAGES], 16)

            def load_weights():
                for c in range(KC):
                    n = P if c < KC - 1 else K_LAST - 1
                    sp.dma_start(w1_sb[0:n, c, :], w1[c * P:c * P + n, :]).then_inc(weights_in, 16)
                sp.dma_start(w1_sb[K_LAST - 1:K_LAST, KC - 1, :], b1).then_inc(weights_in, 16)
                sp.dma_start(w2_sb[:, :, :], w2.rearrange("(c p) n -> p c n", p=P)).then_inc(weights_in, 16)
                sp.dma_start(b2_sb[:, :], b2).then_inc(weights_in, 16)
                sp.dma_start(w3_sb[:, :], w3).then_inc(weights_in, 16)

            def store_y(u, halves=0):
                sp.wait_ge(l3_read, u + halves)
                sp.dma_start(out[bass.ds((u - 1) * MACRO, MACRO), :].rearrange("b o -> o b"),
                             y_row[0:1, :]).then_inc(y_out, 16)

            def macro(m, ids=True):
                if ids:
                    load_ids(m + 2)
                load_index(m + 1, 0)
                if not isinstance(m, int) or m >= 2:
                    store_y(m - 1)
                load_index(m + 1, 1)

            load_index(0, 0)
            load_stage(0)
            load_first_ids(0)
            load_stage(1)
            load_stage(2)
            load_first_ids(1)
            load_index(0, 1)
            load_stage(3)
            load_first_ids(2)
            for k in range(4, NO):
                load_stage(k)
            load_ids(1)
            load_weights()
            macro(0)
            macro(1)
            with sp.Fori(2, MACROS - 2) as m:
                macro(m)
            macro(MACROS - 2, ids=False)
            store_y(MACROS - 2)
            store_y(MACROS - 1)
            store_y(MACROS, halves=1)
            sp.wait_ge(y_out, 16 * MACROS)

        @block.gpsimd
        def _(pool):
            nc.gpsimd.memset(ident[:, :], 0.0).then_inc(zeroed, 1)
            nc.gpsimd.iota(first_row[:, :], pattern=[[0, 1]], base=0, channel_multiplier=CHUNKS,
                           allow_small_or_imprecise_dtypes=True).then_inc(consts_made, 1)
            pool.wait_ge(zeroed, 1)
            nc.gpsimd.affine_select(out=ident[:, :], in_=ident[:, :], compare_op=ALU.not_equal, fill=1.0,
                                    base=0, pattern=[[-1, P]], channel_multiplier=1).then_inc(consts_made, 1)

            def gather_macro(m):
                for h in range(HALVES):
                    pool.wait_ge(index_in[h], m * 16 + 16)
                    if not is_first(m):
                        pool.wait_ge(turned_rows, (m - 1) * (2 * TB) + (h + 1) * TB)
                    pool.sem_inc(gather_open, 1)
                    for g, f in enumerate(gathered):
                        nc.gpsimd.indirect_dma_start(
                            out=rows[h][:, g * DIM:(g + 1) * DIM], out_offset=None, in_=tables[f],
                            in_offset=bass.IndirectOffsetOnAxis(ap=index[h][:, f:f + 1], axis=0),
                        ).then_inc(rows_in[h] if g < EARLY_ROWS else last_rows_in[h], 16)

            over_macros(pool, gather_macro)

        @block.tensor
        def _(pe):
            pe.wait_ge(consts_made, 2)
            pe.wait_ge(pads_set, 3)

            def open_look(m, v):
                pe.wait_ge(look_read, use_before(m, v))
                return look[v % XP]

            def turn_rows(m, h):
                pe.wait_ge(rows_in[h], (m + 1) * (16 * EARLY_ROWS))
                for t in range(TB):
                    if t == TB - 1:
                        pe.wait_ge(last_rows_in[h], (m + 1) * (16 * (NG - EARLY_ROWS)))
                    bank = open_look(m, rows_at(m, h) + t)
                    for g in range(min(4, NG - 4 * t)):
                        at = (4 * t + g) * DIM
                        last = nc.tensor.transpose(bank[:, g * P:(g + 1) * P], rows[h][:, at:at + DIM], ident[:, :])
                    last.then_inc(turned_rows, 1)

            def look_up(m, open_bank, first_table, last_table):
                for x, (k, n, c) in enumerate(STEPS):
                    if not first_table <= k < last_table:
                        continue
                    if c == 0:
                        bank = [open_bank(k + i) for i in range(n)]
                        if is_first(m):
                            pe.wait_ge(lo_made, k + n)
                    pe.wait_ge(hot_made, m * OPM + (x + 1))
                    for i in range(n):
                        seen = hot[x % OHR][0:ROWS_P, i, :]
                        nc.tensor.matmul(bank[i][:, 0:MACRO], table_hi[k + i][0:ROWS_P, c, :], seen,
                                         start=(c == 0), stop=False)
                        last = nc.tensor.matmul(bank[i][:, 0:MACRO], table_lo[k + i][0:ROWS_P, c, :], seen,
                                                start=False, stop=(c == CHUNKS - 1))
                    last.then_inc(hot_used, 1)

            def first_bank_of(k):
                if k >= XP:
                    pe.wait_ge(look_read, k - XP + 1)
                return look[k % XP]

            def products(m, h, first_quad=0, last_quad=QUADS):
                if not (is_first(m) and h == 0) and first_quad == 0:
                    pe.wait_ge(blocks_turned, m * 2 + h)
                for q in range(first_quad, last_quad):
                    bank = prod[:, q // QB, 0:NJ * QB].rearrange("p (j q) -> p j q", q=QB)
                    for s in range(4):
                        last = nc.tensor.matmul(bank[BLOCK * s:BLOCK * s + NI, :, q % QB],
                                                emb[h][:, q, s, 0:NI], emb[h][:, q, s, 1:FEATURES],
                                                start=True, stop=True, tile_position=(0, BLOCK * s))
                if last_quad == QUADS:
                    last.then_inc(prod_full, 1)

            def turn_chunk(c, h, bank, at):
                n = min(P, K1 - c * P)
                return nc.tensor.transpose(bank[0:n, at:at + P], feats[:, h, c * P:c * P + n], ident[:, :])

            def layer1_units(bank, at, n, lo, hi):
                for c in range(KC):
                    k = P if c < KC - 1 else K_LAST
                    done = nc.tensor.matmul(bank[:, at:at + hi - lo], w1_sb[0:k, c, n * P:(n + 1) * P],
                                            feats_t[0:k, c, lo:hi], start=(c == 0), stop=(c == KC - 1))
                return done

            def layer2_units(bank, at, n, lo, hi):
                for c in range(N1):
                    done = nc.tensor.matmul(bank[:, at:at + hi - lo], w2_sb[:, c, n * P:(n + 1) * P],
                                            h1[:, c, lo:hi], start=(c == 0), stop=(c == N1 - 1))
                return done

            def turn_feats(u, first=False):
                pe.wait_ge(pairs_packed, u)
                pe.wait_ge(dense_in, u * 16)
                for c in range(KC):
                    if c == 2 and not first:
                        pe.wait_ge(l3_read, u - 1)
                    for h in range(HALVES):
                        last = turn_chunk(c, h, mlp[c // 2], (c % 2) * MACRO + h * P)
                    if c % 2 == 1 or c == KC - 1:
                        last.then_inc(turned_full, 1)

            def layer1(u):
                pe.wait_ge(turned_read, u * 2)
                for n in range(N1):
                    last = layer1_units(mlp[n // 2], (n % 2) * MACRO, n, 0, MACRO)
                    if n % 2 == 1:
                        last.then_inc(l1_full, 1)

            def layer2(u):
                pe.wait_ge(l1_read, u * 2)
                for n in range(N2):
                    last = layer2_units(mlp[0], n * MACRO, n, 0, MACRO)
                last.then_inc(l2_full, 1)

            def layer3(u):
                pe.wait_ge(h2_weighed, u)
                nc.tensor.matmul(mlp[1][0:1, 0:MACRO], ones[:, :], weighed_h2[:, :],
                                 start=True, stop=True).then_inc(l3_full, 1)

            def turn_half(h):
                pe.wait_ge(pairs_packed, MACROS + h)
                if h == 1:
                    pe.wait_ge(last_packed, 1)
                pe.wait_ge(dense_in, MACROS * 16)
                for c in range(KC):
                    last = turn_chunk(c, h, half_banks[h][0], c * P)
                last.then_inc(turned_full, 1)

            def layer1_half(h):
                pe.wait_ge(turned_read, (MACROS - 1) * 2 + (h + 1))
                for n in range(N1):
                    last = layer1_units(half_banks[h][1], n * P, n, h * P, (h + 1) * P)
                last.then_inc(l1_full, 1)

            def layer2_half(h):
                pe.wait_ge(l1_read, (MACROS - 1) * 2 + (h + 1))
                for n in range(N2):
                    last = layer2_units(half_banks[h][2], n * P, n, h * P, (h + 1) * P)
                last.then_inc(l2_full, 1)

            def layer3_half(h):
                pe.wait_ge(l2_read, MACROS + h)
                for c in range(N2):
                    last = nc.tensor.matmul(half_banks[h][1][0:1, 0:P], w3_sb[:, c:c + 1], h2[:, c, h * P:(h + 1) * P],
                                            start=(c == 0), stop=(c == N2 - 1))
                last.then_inc(l3_full, 1)

            def open_tile1(m):
                pe.wait_ge(look_read, uses(m) + (rows_at(m, 1) + TB))
                pe.wait_ge(joined, m + 1)

            def macro(m):
                first = is_first(m)
                turn_rows(m, 0)
                if not isinstance(m, int) or m >= 2:
                    layer3(m - 1)
                look_up(m + 1, lambda k: open_look(m, table_at(k)), 0, AHEAD)
                pe.wait_ge(look_read, uses(m) + TB)
                products(m, 0)
                if not first:
                    turn_feats(m, isinstance(m, int) and m == 1)
                look_up(m + 1, lambda k: open_look(m, table_at(k)), AHEAD, EARLY)
                if not first:
                    if isinstance(m, int):
                        pe.wait_ge(weights_in, 16 * N_WEIGHTS)
                    layer1(m)
                turn_rows(m, 1)
                if not first:
                    layer2(m)
                look_up(m + 1, lambda k: open_look(m, table_at(k)), EARLY, NO)
                open_tile1(m)
                products(m, 1)

            def last_macro(m):
                turn_rows(m, 0)
                layer3(m - 1)
                pe.wait_ge(look_read, uses(m) + TB)
                products(m, 0, 0, QUADS // 2)
                turn_feats(m)
                products(m, 0, QUADS // 2, QUADS)
                layer1(m)
                layer2(m)
                turn_rows(m, 1)
                turn_half(0)
                open_tile1(m)
                products(m, 1)
                pe.wait_ge(l2_read, m)
                layer1_half(0)
                layer3(m)
                turn_half(1)
                layer2_half(0)
                layer1_half(1)
                layer3_half(0)
                layer2_half(1)
                layer3_half(1)

            look_up(0, first_bank_of, 0, NO)
            over_macros(pe, macro, last_macro)

        def pack(copy, halves, j):
            at = j * (j - 1) // 2
            return copy(feats[:, halves[0]:halves[1], at:at + j], byj[:, halves[0]:halves[1], j - 1, 0:j])

        @block.scalar
        def _(act):
            def load_dense(m):
                if not is_first(m):
                    act.wait_ge(turned_full, m * 2)
                act.dma_start(feats[:, :, PAIRS:PAIRS + DENSE],
                              dense[bass.ds(m * MACRO, MACRO), :].rearrange("(h p) e -> p h e", p=P)
                              ).then_inc(dense_in, 16)

            def round_tables(k, n):
                for t in range(k, k + n):
                    act.wait_ge(stage_in[t % STAGES], 16 * (t // STAGES + 1))
                    nc.scalar.copy(table_hi[t][0:ROWS_P, :, :], stage[t % STAGES][0:ROWS_P, :, :]).then_inc(hi_made, 1)

            def copy_turned(m, h):
                for t in range(TB):
                    n = min(4, NG - 4 * t)
                    act.wait_ge(turned_rows, m * (2 * TB) + (h * TB + t + 1))
                    nc.scalar.copy(emb[h][:, :, :, 4 * t:4 * t + n].rearrange("p q s f -> p f s q"),
                                   look[(rows_at(m, h) + t) % XP][:, 0:n * P].rearrange("p (f s q) -> p f s q", s=4, q=QUADS)
                                   ).then_inc(look_read, 1)

            def copy_looked_up(m, bank_of, first_table, last_table):
                if first_table == 0 and not is_first(m):
                    act.wait_ge(joined, m)
                    act.wait_ge(prod_full, m * 2 - 1)
                for g, (k, n) in enumerate(GROUPS):
                    if not first_table <= k < last_table:
                        continue
                    if is_first(m) and g + 2 < len(GROUPS):
                        round_tables(*GROUPS[g + 2])
                    act.wait_ge(hot_used, m * OPM + (g + 1) * CHUNKS)
                    for i in range(k, k + n):
                        bank = look[bank_of(i) % XP]
                        nc.scalar.copy(emb[0][:, :, :, NG + i].rearrange("p q s -> p s q"),
                                       bank[:, 0:P].rearrange("p (s q) -> p s q", s=4))
                        nc.scalar.copy(waiting[:, i, :], bank[:, P:MACRO]).then_inc(look_read, 1)

            def relu1(u):
                for i in range(2):
                    act.wait_ge(l1_full, u * 2 + (i - 1))
                    nc.scalar.activation(h1[:, 2 * i:2 * i + 2, :].rearrange("p n b -> p (n b)"),
                                         mlp[i][:, :], ACT.Relu).then_inc(l1_read, 1)

            def relu2(u):
                if not (isinstance(u, int) and u == 1):
                    act.wait_ge(h2_weighed, u - 1)
                act.wait_ge(l2_full, u)
                for n in range(N2):
                    done = nc.scalar.activation(h2[:, n, :], mlp[0][:, n * MACRO:(n + 1) * MACRO], ACT.Relu,
                                                bias=b2_sb[:, n:n + 1])
                done.then_inc(l2_read, 1)

            def relu1_half(h):
                act.wait_ge(l1_full, (MACROS - 1) * 2 + (h + 1))
                nc.scalar.activation(h1[:, :, h * P:(h + 1) * P],
                                     half_banks[h][1][:, 0:N1 * P].rearrange("p (n b) -> p n b", n=N1),
                                     ACT.Relu).then_inc(l1_read, 1)

            def relu2_half(h):
                act.wait_ge(h2_weighed, MACROS - 1)
                act.wait_ge(l2_full, MACROS + h)
                for n in range(N2):
                    done = nc.scalar.activation(h2[:, n, h * P:(h + 1) * P], half_banks[h][2][:, n * P:(n + 1) * P],
                                                ACT.Relu, bias=b2_sb[:, n:n + 1])
                done.then_inc(l2_read, 1)

            def macro(m):
                first = is_first(m)
                copy_turned(m, 0)
                if not first:
                    load_dense(m)
                copy_looked_up(m + 1, table_at, 0, EARLY)
                if not first:
                    relu1(m)
                copy_turned(m, 1)
                if not first:
                    if isinstance(m, int):
                        act.wait_ge(weights_in, 16 * N_WEIGHTS)
                    relu2(m)
                copy_looked_up(m + 1, table_at, EARLY, NO)

            def last_macro(m):
                copy_turned(m, 0)
                load_dense(m)
                relu1(m)
                copy_turned(m, 1)
                relu2(m)
                act.wait_ge(blocks_turned, MACROS * 2)
                for j in range(ACT_PACKS, NJ + 1):
                    done = pack(nc.scalar.copy, (1, 2), j)
                done.then_inc(last_packed, 1)
                for h in range(HALVES):
                    relu1_half(h)
                    relu2_half(h)

            load_dense(0)
            for group in GROUPS[:2]:
                round_tables(*group)
            copy_looked_up(0, lambda k: k, 0, NO)
            over_macros(act, macro, last_macro)

        @block.vector
        def _(dve):
            nc.vector.memset(prod[:, :, :], 0.0).then_inc(pads_set, 1)
            nc.vector.memset(feats[:, :, K1 - 1:K1], 1.0).then_inc(pads_set, 1)
            nc.vector.memset(ones[:, :], 1.0).then_inc(pads_set, 1)
            dve.wait_ge(consts_made, 2)

            def compare_from(tables, made):
                first, last = tables
                nc.vector.tensor_scalar(id_steps[0:ROWS_P, first:last, :], id_rows[0:ROWS_P, first:last, :],
                                        first_row[0:ROWS_P, 0:1], None, ALU.subtract).then_inc(steps_made, 1)
                dve.wait_ge(steps_made, made)

            def make_first_steps(i):
                if i < len(ID_PARTS) - 1:
                    dve.wait_ge(first_ids_in[i], 16)
                else:
                    dve.wait_ge(ids_in, 16)
                compare_from(ID_PARTS[i], i + 1)

            def make_steps(m):
                dve.wait_ge(ids_in, m * 16 + 16)
                dve.wait_ge(hot_made, m * OPM)
                compare_from((0, NO), m + len(ID_PARTS))

            def make_rest(k, n):
                for t in range(k, k + n):
                    dve.wait_ge(hi_made, t + 1)
                    nc.vector.tensor_tensor(table_lo[t][0:ROWS_P, :, :], stage[t % STAGES][0:ROWS_P, :, :],
                                            table_hi[t][0:ROWS_P, :, :].bitcast(f32),
                                            ALU.subtract).then_inc(lo_made, 1)

            def make_hot(m, first_step, last_step):
                for x in range(first_step, last_step):
                    k, n, c = STEPS[x]
                    if is_first(m) and c == 0:
                        make_rest(k, n)
                        for i, (first, _) in enumerate(ID_PARTS):
                            if k == first:
                                make_first_steps(i)
                    if not (is_first(m) and x < OHR):
                        dve.wait_ge(hot_used, m * OPM + (x - OHR + 1))
                    nc.vector.tensor_scalar(hot[x % OHR][0:ROWS_P, 0:n, :], id_steps[0:ROWS_P, k:k + n, :],
                                            float(c), None, ALU.is_equal).then_inc(hot_made, 1)

            def copy_feats_t(u):
                dve.wait_ge(turned_full, u * 2 - 1)
                nc.vector.tensor_copy(feats_t[:, 0:2, :].rearrange("p c b -> p (c b)"), mlp[0][:, :]).then_inc(turned_read, 1)
                dve.wait_ge(turned_full, u * 2)
                nc.vector.tensor_copy(feats_t[0:K_LAST, 2, :], mlp[1][0:K_LAST, 0:MACRO]).then_inc(turned_read, 1)

            def copy_half(h):
                dve.wait_ge(turned_full, (MACROS - 1) * 2 + (h + 1))
                bank = half_banks[h][0]
                nc.vector.tensor_copy(feats_t[:, 0:2, h * P:(h + 1) * P],
                                      bank[:, 0:2 * P].rearrange("p (c b) -> p c b", c=2))
                nc.vector.tensor_copy(feats_t[0:K_LAST, 2, h * P:(h + 1) * P],
                                      bank[0:K_LAST, 2 * P:3 * P]).then_inc(turned_read, 1)

            def turn_blocks(m, h):
                dve.wait_ge(prod_full, m * 2 + (h + 1))
                if h == 0 and not is_first(m):
                    dve.wait_ge(pairs_packed, m)
                nc.vector.transpose(byj[:, h, :, :],
                                    prod[:, :, 0:NJ * QB].rearrange("p b (j q) -> p j b q", q=QB)
                                    ).then_inc(blocks_turned, 1)

            def pack_pairs(tiles, halves, end):
                dve.wait_ge(blocks_turned, tiles)
                for j in range(1, end):
                    done = pack(nc.vector.tensor_copy, halves, j)
                done.then_inc(pairs_packed, 1)

            def join_waiting(m):
                dve.wait_ge(look_read, uses(m))
                if not is_first(m):
                    dve.wait_ge(prod_full, m * 2)
                nc.vector.tensor_copy(emb[1][:, :, :, NG:FEATURES].rearrange("p q s f -> p f s q"),
                                      waiting[:, :, :].rearrange("p f (s q) -> p f s q", s=4)).then_inc(joined, 1)

            def weigh_h2(u):
                dve.wait_ge(l2_read, u)
                nc.vector.tensor_scalar(weighed_h2[:, :], h2[:, 0, :], w3_sb[:, 0:1], None, ALU.mult
                                        ).then_inc(h2_half_weighed, 1)
                dve.wait_ge(h2_half_weighed, u)
                nc.vector.scalar_tensor_tensor(weighed_h2[:, :], h2[:, 1, :], w3_sb[:, 1:2], weighed_h2[:, :],
                                               ALU.mult, ALU.add).then_inc(h2_weighed, 1)

            def copy_y(u, first=False):
                if not first:
                    dve.wait_ge(y_out, u * 16 - 16)
                dve.wait_ge(l3_full, u)
                nc.vector.tensor_copy(y_row[0:1, :], mlp[1][0:1, 0:MACRO]).then_inc(l3_read, 1)

            def copy_half_y(h):
                dve.wait_ge(l3_full, MACROS + h)
                if h == 0:
                    dve.wait_ge(y_out, (MACROS - 1) * 16)
                nc.vector.tensor_copy(y_row[0:1, h * P:(h + 1) * P], half_banks[h][1][0:1, 0:P]).then_inc(l3_read, 1)

            def start_macro(m):
                if not is_first(m):
                    turn_blocks(m - 1, 1)
                    pack_pairs(m * 2, (0, 2), NJ + 1)
                if not isinstance(m, int) or m >= 2:
                    copy_y(m - 1, isinstance(m, int) and m == 2)
                join_waiting(m)
                if not is_last(m):
                    make_hot(m + 1, HEAD, MIDDLE)
                if not is_first(m):
                    copy_feats_t(m)

            def macro(m, steps=True):
                start_macro(m)
                turn_blocks(m, 0)
                make_hot(m + 1, MIDDLE, OPM)
                if not is_first(m):
                    weigh_h2(m)
                if steps:
                    make_steps(m + 2)
                    make_hot(m + 2, 0, HEAD)

            make_hot(0, 0, OPM)
            make_steps(1)
            make_hot(1, 0, HEAD)
            for m in range(3):
                macro(m)
            with dve.Fori(3, MACROS - 2) as m:
                macro(m)
            macro(MACROS - 2, steps=False)
            start_macro(MACROS - 1)
            turn_blocks(MACROS - 1, 0)
            pack_pairs(MACROS * 2 - 1, (0, 1), NJ + 1)
            copy_half(0)
            weigh_h2(MACROS - 1)
            turn_blocks(MACROS - 1, 1)
            pack_pairs(MACROS * 2, (1, 2), ACT_PACKS)
            copy_half(1)
            copy_y(MACROS - 1)
            copy_half_y(0)
            copy_half_y(1)


def kernel(**inputs):
    import concourse.bacc as bacc
    from concourse.bass_utils import run_bass_kernel_spmd

    nc = bacc.Bacc("TRN2", target_bir_lowering=False, num_devices=1)
    arrays = {}

    def give(name, array):
        array = np.ascontiguousarray(array)
        arrays[f"in_{name}"] = array
        return nc.dram_tensor(f"in_{name}", array.shape, mybir.dt.from_np(array.dtype), kind="ExternalInput").ap()

    tables = [np.asarray(inputs[f"tbl_{f}"]) for f in range(FEATURES)]
    gathered, one_hot = feature_order([t.shape[0] for t in tables])
    w1 = np.asarray(inputs["W_top1"])
    pairs = FEATURES * (FEATURES - 1) // 2
    rows = pair_rows(gathered + one_hot) + list(range(pairs, w1.shape[0]))
    ids = np.asarray(inputs["ids"])
    out = nc.dram_tensor("out_0", (ids.shape[0], 1), mybir.dt.float32, kind="ExternalOutput").ap()
    ids_t = ids[:, one_hot].reshape(-1, MACRO, len(one_hot)).transpose(0, 2, 1)
    build(nc, give("dense", inputs["dense_ctx"]), give("ids", ids), give("ids_t", ids_t),
          [give(f"tbl_{f}", t) for f, t in enumerate(tables)],
          give("w1", w1[rows]), give("b1", np.asarray(inputs["b_top1"]).reshape(1, -1)),
          give("w2", inputs["W_top2"]), give("b2", np.asarray(inputs["b_top2"]).reshape(-1, P).T),
          give("w3", np.asarray(inputs["W_top3"]).reshape(-1, P).T), out)
    return run_bass_kernel_spmd(nc, [arrays], core_ids=[0]).results[0]["out_0"]
```
